# Optimizing a Trainium2 kernel written in Bass

```python
import numpy as np
import jax
import jax.numpy as jnp

def _softmax(x, axis=-1):
    return jax.nn.softmax(x, axis=axis)

def _gelu(x):
    return jax.nn.gelu(x, approximate=True)

def _silu(x):
    return jax.nn.silu(x)

def _sigmoid(x):
    return jax.nn.sigmoid(x)

def _layernorm(x, axis=-1, eps=1e-05):
    m = jnp.mean(x, axis=axis, keepdims=True)
    v = jnp.var(x, axis=axis, keepdims=True)
    return (x - m) / jnp.sqrt(v + eps)

def _scatter_add(tgt, idx, src, axis=0):
    return tgt.at[idx].add(src)

def _segment_sum(src, seg, n):
    return jax.ops.segment_sum(src, seg, n)
kernel_name = 'mk_gnn_resnorm_d1_gnn_r8_8ea0ef'

def setup_inputs(seed: int=0):
    np.random.seed(seed)
    _w = jnp.asarray

    def _rec_inputs():
        import jax
        import jax.numpy as jnp
        _gk = jax.random.key(seed)
        x = -0.0001006 + 1 * jax.random.normal(jax.random.fold_in(_gk, 1), (6250, 96), jnp.float32)
        src = jax.random.randint(jax.random.fold_in(_gk, 2), (100000,), 0, 6250, jnp.int32)
        dst = jax.random.randint(jax.random.fold_in(_gk, 3), (100000,), 0, 6250, jnp.int32)
        _o = jnp.argsort(dst, stable=True)
        src = src[_o]
        dst = dst[_o]
        edge_attr_96 = 5.93493e-05 + 1.00006 * jax.random.normal(jax.random.fold_in(_gk, 11), (100000, 96), jnp.float32)
        return (x, src, dst, edge_attr_96)
    x, src, dst, edge_attr_96 = _rec_inputs()

    def _L0_gnn_setup():
        import jax, jax.numpy as jnp
        import numpy as np
        N_NODES = 6250
        N_EDGES = 100000
        NIN = 96
        NOUT = 96
        key = jax.random.key(seed)
        ks = jax.random.split(key, 10)
        s = 1.0 / np.sqrt(NIN)
        so = 1.0 / np.sqrt(NOUT)
        return {'x': jax.random.normal(ks[0], (N_NODES, NIN), dtype=jnp.float32), 'edge_index': jax.random.randint(ks[1], (2, N_EDGES), 0, N_NODES, dtype=jnp.int64), 'edge_attr': jax.random.normal(ks[2], (N_EDGES, NIN), dtype=jnp.float32), 'W_edge': jax.random.uniform(ks[3], (NIN, NIN), jnp.float32, -s, s), 'b_edge': jax.random.uniform(ks[4], (NIN,), jnp.float32, -s, s), 'eps': jnp.zeros((), dtype=jnp.float32), 'W1': jax.random.uniform(ks[5], (NOUT, NIN), jnp.float32, -s, s), 'b1': jax.random.uniform(ks[6], (NOUT,), jnp.float32, -s, s), 'W2': jax.random.uniform(ks[7], (NOUT, NOUT), jnp.float32, -so, so), 'b2': jax.random.uniform(ks[8], (NOUT,), jnp.float32, -so, so)}
    _L0_gnn_all = _L0_gnn_setup()
    _L0_gnn_in = {k: v for k, v in _L0_gnn_all.items() if k in ('W_edge', 'b_edge', 'eps', 'W1', 'b1', 'W2', 'b2')}
    del _L0_gnn_all
    return {'x': x, 'src': src, 'dst': dst, 'edge_attr_96': edge_attr_96, 'L0_gnn_W_edge': _L0_gnn_in['W_edge'], 'L0_gnn_b_edge': _L0_gnn_in['b_edge'], 'L0_gnn_eps': _L0_gnn_in['eps'], 'L0_gnn_W1': _L0_gnn_in['W1'], 'L0_gnn_b1': _L0_gnn_in['b1'], 'L0_gnn_W2': _L0_gnn_in['W2'], 'L0_gnn_b2': _L0_gnn_in['b2']}

def reference(x, src, dst, edge_attr_96, L0_gnn_W_edge, L0_gnn_b_edge, L0_gnn_eps, L0_gnn_W1, L0_gnn_b1, L0_gnn_W2, L0_gnn_b2):
    import jax
    import jax.numpy as jnp

    def _L0_gnn_ref(x, edge_index, edge_attr, W_edge, b_edge, eps, W1, b1, W2, b2):
        import jax, jax.numpy as jnp
        import numpy as np
        N_NODES = 6250
        N_EDGES = 100000
        NIN = 96
        NOUT = 96
        ea = edge_attr @ W_edge.T + b_edge
        src, dst = (edge_index[0], edge_index[1])
        msg = jax.nn.relu(x[src] + ea)
        aggr = jax.ops.segment_sum(msg, dst, num_segments=N_NODES)
        h = (1.0 + eps) * x + aggr
        h = jax.nn.relu(h @ W1.T + b1)
        return h @ W2.T + b2
    edge_index = jnp.stack([src, dst])
    x = _layernorm(x + _L0_gnn_ref(x, edge_index, edge_attr_96, L0_gnn_W_edge, L0_gnn_b_edge, L0_gnn_eps, L0_gnn_W1, L0_gnn_b1, L0_gnn_W2, L0_gnn_b2), axis=-1)
    return x

_drawn_inputs = setup_inputs


def setup_inputs(seed=0):
    import zlib

    import numpy as np

    out = dict(_drawn_inputs(seed))
    spreads = {}
    factors = {'L0_gnn_b1': 4.893}
    for name, (base, spread) in spreads.items():
        noise = np.random.default_rng([zlib.crc32(name.encode()), seed]).standard_normal(out[name].shape)
        drawn = base * np.exp(spread * noise) if base else spread * noise
        out[name] = jnp.asarray(drawn.astype(out[name].dtype))
    for name, factor in factors.items():
        out[name] = (out[name] * factor).astype(out[name].dtype)
    return out
```

```python
from contextlib import ExitStack

import concourse.bass as bass
from concourse import mybir

F32 = mybir.dt.float32
I32 = mybir.dt.int32
ALU = mybir.AluOpType
ACT = mybir.ActivationFunctionType
AX_X = mybir.AxisListType.X

P = 128
K = 8
HALF = 4
W = 128
SLOTS = 4
LN_EPS = 1e-5


def build_gnn(nc, x, src, dst, edge_attr, w_edge, b_edge, eps, w1, b1, w2, b2, out):
    N, F = x.shape
    E = src.shape[0]
    CHUNK = P * K
    FULL = E // CHUNK
    REST = E - FULL * CHUNK
    KL = 6
    PL = REST // KL
    CHUNKS = FULL + 1
    ROUNDS = FULL // SLOTS
    assert PL * KL == REST and PL <= P and PL % 16 == 0 and CHUNKS <= P
    NB = -(-N // P)
    NREST = N - (NB - 1) * P
    GROUPS = -(-NB // HALF)

    def shape_of(t):
        return (PL, KL) if isinstance(t, int) and t == CHUNKS - 1 else (P, K)

    with ExitStack() as ctx:
        def sb(name, shape, dt=F32):
            return ctx.enter_context(nc.sbuf_tensor(name, shape, dt))

        def ps(name, shape=(P, 512)):
            return ctx.enter_context(nc.psum_tensor(name, list(shape), F32))

        def sem(name):
            return ctx.enter_context(nc.semaphore(name))

        src_idx = [sb(f"src_idx{s}", [P, K], I32) for s in range(SLOTS)]
        dst_idx = [sb(f"dst_idx{s}", [P, K], I32) for s in range(SLOTS)]
        attr = [sb(f"attr{s}", [P, K, F]) for s in range(SLOTS)]
        x_src = [sb(f"x_src{s}", [P, K, F]) for s in range(SLOTS)]
        attr_t = [sb(f"attr_t{h}", [F + 1, HALF * P]) for h in range(2)]
        msg = [sb(f"msg{m}", [P, K, F]) for m in range(2)]
        dst_f = sb("dst_f", [P, K])
        dst_rel = sb("dst_rel", [P, K])
        onehot = sb("onehot", [P, K, W])
        sums_t = sb("sums_t", [F, N + W])
        x_rows = sb("x_rows", [P, NB, F])
        dst_rows = sb("dst_rows", [CHUNKS, CHUNK], I32)
        dst_off = sb("dst_off", [CHUNKS, CHUNK])
        off_max = sb("off_max", [CHUNKS, 1])
        off_min = sb("off_min", [CHUNKS, 1])
        over = sb("over", [CHUNKS, 1])
        under = sb("under", [CHUNKS, 1])
        outside = sb("outside", [CHUNKS, 1])
        first_wide = sb("first_wide", [CHUNKS, P])
        chunk_base = sb("chunk_base", [P, CHUNKS])
        chunk_base_i = sb("chunk_base_i", [1, CHUNKS], I32)
        spread_i = sb("spread_i", [1, 1], I32)
        window_base_i = sb("window_base_i", [P, NB], I32)
        window_base = sb("window_base", [P, NB])
        col_i = sb("col_i", [P, P], I32)
        row_i = sb("row_i", [P, 1], I32)
        ident = sb("ident", [P, P])
        ones = sb("ones", [P, 1])
        w_in = [sb(f"w_in{j}", [F, F]) for j in range(3)]
        w_edge_t = sb("w_edge_t", [F + 1, F])
        w1_t = sb("w1_t", [F, F])
        w2_t = sb("w2_t", [F + 1, F])
        b1_col = sb("b1_col", [F, 1])
        eps_col = sb("eps_col", [F, 1])
        eps1_col = sb("eps1_col", [F, 1])
        hid_t = [sb(f"hid_t{j}", [F + 1, HALF * P]) for j in range(2)]
        res = [sb(f"res{j}", [P, HALF, F]) for j in range(2)]
        stats = sb("stats", [P, HALF, 6])
        mean_var = [sb(f"mean_var{j}", [P, HALF, 2]) for j in range(2)]
        ln_eps = sb("ln_eps", [P, 1])
        std = [sb(f"std{j}", [P, HALF]) for j in range(2)]
        rstd = [sb(f"rstd{j}", [P, HALF]) for j in range(2)]
        y = [sb(f"y{j}", [P, HALF, F]) for j in range(2)]

        tp = [ps(f"tp{h}") for h in range(2)]
        ep = [ps(f"ep{h}") for h in range(2)]
        win = [ps(f"win{j}") for j in range(2)]
        col_f = ps("col_f", (P, P))
        small = ps("small")

        src_loaded = [sem(f"src_loaded{s}") for s in range(SLOTS)]
        dst_loaded = [sem(f"dst_loaded{s}") for s in range(SLOTS)]
        attr_loaded = [sem(f"attr_loaded{s}") for s in range(SLOTS)]
        gathered = [sem(f"gathered{s}") for s in range(SLOTS)]
        sp_steps = sem("sp_steps")
        pool_steps = sem("pool_steps")
        rows_loaded = sem("rows_loaded")
        weights_loaded = sem("weights_loaded")
        bias_loaded = sem("bias_loaded")
        x_loaded = sem("x_loaded")
        iotas_made = sem("iotas_made")
        consts = sem("consts")
        ident_made = sem("ident_made")
        flagged = sem("flagged")
        flag_summed = sem("flag_summed")
        flag_ready = sem("flag_ready")
        w_turned = sem("w_turned")
        w_ready = sem("w_ready")
        eps_ready = sem("eps_ready")
        x_turned = sem("x_turned")
        sums_begun = sem("sums_begun")
        turned = sem("turned")
        copied = sem("copied")
        projected = sem("projected")
        added = sem("added")
        relued = sem("relued")
        dst_taken = sem("dst_taken")
        rel_made = sem("rel_made")
        onehot_made = sem("onehot_made")
        window_summed = sem("window_summed")
        window_added = sem("window_added")
        sums_done = sem("sums_done")
        hid_done = sem("hid_done")
        hid_ready = sem("hid_ready")
        mlp_done = sem("mlp_done")
        res_ready = sem("res_ready")
        stats_ready = sem("stats_ready")
        norm_chain = sem("norm_chain")
        std_ready = sem("std_ready")
        y_ready = sem("y_ready")
        stored = [sem(f"stored{j}") for j in range(2)]

        CONSTS = 9
        LAST_START = E - CHUNK
        block_nodes = [min(P, N - b * P) for b in range(NB)]
        group_blocks = [range(g * HALF, min(NB, g * HALF + HALF)) for g in range(GROUPS)]
        group_rows = [block_nodes[blocks[0]] for blocks in group_blocks]
        assert all(block_nodes[b] == r for blocks, r in zip(group_blocks, group_rows) for b in blocks)
        group_cols = [sum(block_nodes[b] for b in blocks) for blocks in group_blocks]

        block = ctx.enter_context(nc.Block())

        @block.sync
        def _(sp):
            def load(start, s, pc, kc):
                n = pc * kc
                sp.dma_start(src_idx[s][0:pc, 0:kc],
                             src[bass.ds(start, n)].rearrange("(p k) -> p k", k=kc)).then_inc(src_loaded[s], 16)
                sp.dma_start(dst_idx[s][0:pc, 0:kc],
                             dst[bass.ds(start, n)].rearrange("(p k) -> p k", k=kc)).then_inc(dst_loaded[s], 16)
                sp.dma_start(attr[s][0:pc, 0:kc, :],
                             edge_attr[bass.ds(start, n), :].rearrange("(p k) f -> p k f", k=kc)
                             ).then_inc(attr_loaded[s], 16)

            for s in range(SLOTS):
                load(s * CHUNK, s, P, K)
            with sp.Fori(1, ROUNDS) as i:
                for s in range(SLOTS):
                    start = sp.snap(i * (SLOTS * CHUNK) + s * CHUNK)
                    sp.wait_ge(gathered[s], i * (16 * K))
                    sp.sem_inc(sp_steps, 1)
                    sp.wait_ge(turned, i * (2 * SLOTS) + (2 * (s - SLOTS) + 2))
                    sp.sem_inc(sp_steps, 1)
                    sp.wait_ge(dst_taken, i * SLOTS + (s - SLOTS + 1))
                    sp.sem_inc(sp_steps, 1)
                    load(start, s, P, K)
            for t in range(ROUNDS * SLOTS, CHUNKS):
                s, u = t % SLOTS, t - SLOTS
                sp.wait_ge(gathered[s], 16 * K * (t // SLOTS))
                sp.wait_ge(turned, 2 * u + 2)
                sp.wait_ge(dst_taken, u + 1)
                load(t * CHUNK, s, *shape_of(t))

            blocks_done = 0
            for g, blocks in enumerate(group_blocks):
                n, pg, b0 = len(blocks), group_rows[g], blocks[0]
                blocks_done += n
                sp.wait_ge(y_ready, blocks_done)
                sp.dma_start(out[b0 * P:b0 * P + n * pg, :].rearrange("(b p) f -> p b f", p=pg),
                             y[g % 2][0:pg, 0:n, :]).then_inc(stored[g % 2], 16)
            for j in range(2):
                sp.wait_ge(stored[j], 16 * sum(1 for g in range(GROUPS) if g % 2 == j))

        @block.gpsimd
        def _(pool):
            nc.gpsimd.iota(col_i[:], pattern=[[1, P]], base=0, channel_multiplier=0).then_inc(iotas_made, 1)
            nc.gpsimd.iota(row_i[:], pattern=[[0, 1]], base=0, channel_multiplier=1).then_inc(iotas_made, 1)
            nc.gpsimd.iota(window_base_i[:], pattern=[[W, NB]], base=0, channel_multiplier=0).then_inc(iotas_made, 1)

            def gather(s, pc, kc):
                for k in range(kc):
                    nc.gpsimd.indirect_dma_start(
                        out=x_src[s][0:pc, k, :], out_offset=None, in_=x,
                        in_offset=bass.IndirectOffsetOnAxis(ap=src_idx[s][0:pc, k:k + 1], axis=0),
                    ).then_inc(gathered[s], 16)

            for s in range(SLOTS):
                pool.wait_ge(src_loaded[s], 16)
                gather(s, P, K)
            with pool.Fori(1, ROUNDS) as i:
                for s in range(SLOTS):
                    pool.wait_ge(added, i * (2 * SLOTS) + (2 * (s - SLOTS) + 2))
                    pool.wait_ge(src_loaded[s], i * 16 + 16)
                    pool.sem_inc(pool_steps, 1)
                    gather(s, P, K)
            for t in range(ROUNDS * SLOTS, CHUNKS):
                s = t % SLOTS
                pool.wait_ge(added, 2 * (t - SLOTS) + 2)
                pool.wait_ge(src_loaded[s], 16 * (t // SLOTS + 1))
                gather(s, *shape_of(t))

        @block.scalar
        def _(act):
            act.dma_start(dst_rows[0:FULL, :], dst[0:FULL * CHUNK].rearrange("(t e) -> t e", e=CHUNK)
                          ).then_inc(rows_loaded, 16)
            act.dma_start(dst_rows[FULL:CHUNKS, :], dst[LAST_START:E].rearrange("(t e) -> t e", e=CHUNK)
                          ).then_inc(rows_loaded, 16)
            for j, w in enumerate((w_edge, w1, w2)):
                act.dma_start(w_in[j][:], w).then_inc(weights_loaded, 16)
            act.dma_start(w_edge_t[F:F + 1, :], b_edge.rearrange("(a f) -> a f", a=1)).then_inc(bias_loaded, 16)
            act.dma_start(w2_t[F:F + 1, :], b2.rearrange("(a f) -> a f", a=1)).then_inc(bias_loaded, 16)
            act.dma_start(b1_col[:], b1.rearrange("(f a) -> f a", a=1)).then_inc(bias_loaded, 16)
            act.dma_start(eps_col[:], eps.rearrange("(a b) -> a b", a=1).to_broadcast([F, 1])).then_inc(bias_loaded, 16)
            act.dma_start(x_rows[:, 0:NB - 1, :], x[0:(NB - 1) * P, :].rearrange("(b p) f -> p b f", p=P)
                          ).then_inc(x_loaded, 16)
            act.dma_start(x_rows[0:NREST, NB - 1, :], x[(NB - 1) * P:N, :]).then_inc(x_loaded, 16)

            act.wait_ge(eps_ready, 1)
            for g in range(GROUPS):
                act.wait_ge(x_turned, g + 1)
                nc.scalar.activation(sums_t[:, g * HALF * P:g * HALF * P + group_cols[g]],
                                     tp[g % 2][0:F, 0:group_cols[g]], ACT.Copy,
                                     scale=eps1_col[:, 0:1]).then_inc(sums_begun, 1)

            def copy_half(t, h):
                pc, kc = shape_of(t)
                n = min(kc - h * HALF, HALF)
                act.wait_ge(turned, 2 * t + (h + 1))
                if not isinstance(t, int) or t > 0:
                    act.wait_ge(projected, 2 * t + (h - 1))
                nc.scalar.activation(
                    attr_t[h][0:F, :].rearrange("f (k p) -> f k p", p=P)[:, 0:n, 0:pc],
                    tp[h][0:F, :].rearrange("f (k p) -> f k p", p=P)[:, 0:n, 0:pc],
                    ACT.Copy).then_inc(copied, 1)

            def relu_half(t, m, h):
                pc, kc = shape_of(t)
                k0, k1 = h * HALF, min(kc, h * HALF + HALF)
                act.wait_ge(added, 2 * t + (h + 1))
                nc.scalar.activation(msg[m][0:pc, k0:k1, :], msg[m][0:pc, k0:k1, :], ACT.Relu).then_inc(relued, 1)

            def step(t, parity):
                copy_half(t, 0)
                copy_half(t, 1)
                if not isinstance(t, int) or t > 0:
                    relu_half(t - 1, 1 - parity, 0)
                    relu_half(t - 1, 1 - parity, 1)

            for t in range(SLOTS):
                step(t, t % 2)
            with act.Fori(1, ROUNDS) as i:
                for s in range(SLOTS):
                    step(i * SLOTS + s, s % 2)
            for t in range(ROUNDS * SLOTS, CHUNKS):
                step(t, t % 2)
            relu_half(CHUNKS - 1, (CHUNKS - 1) % 2, 0)
            relu_half(CHUNKS - 1, (CHUNKS - 1) % 2, 1)

            def hidden(g):
                act.wait_ge(hid_done, g + 1)
                if g >= 2:
                    act.wait_ge(mlp_done, g - 1)
                nc.scalar.activation(hid_t[g % 2][0:F, 0:group_cols[g]], tp[g % 2][0:F, 0:group_cols[g]],
                                     ACT.Relu, bias=b1_col[:, 0:1]).then_inc(hid_ready, 1)

            def norm(g):
                n, pg, j = len(group_blocks[g]), group_rows[g], g % 2
                act.wait_ge(stats_ready, g * HALF + n)
                nc.scalar.activation(std[j][0:pg, 0:n], mean_var[j][0:pg, 0:n, 1], ACT.Sqrt,
                                     bias=ln_eps[0:pg, 0:1]).then_inc(std_ready, 1)

            for g in range(GROUPS + 1):
                if g < GROUPS:
                    hidden(g)
                if g >= 1:
                    norm(g - 1)

        @block.vector
        def _(dve):
            nc.vector.memset(ones[:], 1.0).then_inc(consts, 1)
            nc.vector.memset(ln_eps[:], LN_EPS).then_inc(consts, 1)
            for a in (attr_t[0], attr_t[1], hid_t[0], hid_t[1]):
                nc.vector.memset(a[F:F + 1, :], 1.0).then_inc(consts, 1)
            nc.vector.memset(sums_t[:, N:N + W], 0.0).then_inc(consts, 1)
            dve.wait_ge(iotas_made, 3)
            nc.vector.tensor_tensor(ident[:], col_i[:], row_i[:].to_broadcast([P, P]),
                                    ALU.is_equal).then_inc(ident_made, 1)
            nc.vector.tensor_copy(col_f[:], col_i[:]).then_inc(consts, 1)
            nc.vector.tensor_copy(window_base[:], window_base_i[:]).then_inc(consts, 1)

            dve.wait_ge(rows_loaded, 32)
            nc.vector.tensor_tensor(dst_off[:], dst_rows[:], dst_rows[:, 0:1].to_broadcast([CHUNKS, CHUNK]),
                                    ALU.subtract).then_inc(flagged, 1)
            nc.vector.tensor_copy(first_wide[:], dst_rows[:, 0:1].to_broadcast([CHUNKS, P])).then_inc(flagged, 1)
            dve.wait_ge(flagged, 2)
            nc.vector.tensor_reduce(off_max[:], dst_off[:], AX_X, ALU.max).then_inc(flagged, 1)
            nc.vector.tensor_reduce(off_min[:], dst_off[:], AX_X, ALU.min).then_inc(flagged, 1)
            dve.wait_ge(flagged, 4)
            nc.vector.tensor_scalar(over[:], off_max[:], float(W - 1), None, ALU.is_gt).then_inc(flagged, 1)
            nc.vector.tensor_scalar(under[:], off_min[:], 0.0, None, ALU.is_lt).then_inc(flagged, 1)
            dve.wait_ge(flagged, 6)
            nc.vector.tensor_tensor(outside[:], over[:], under[:], ALU.add).then_inc(flagged, 1)
            dve.wait_ge(flag_summed, 1)
            nc.vector.tensor_copy(spread_i[:], small[0:1, 0:1]).then_inc(flag_ready, 1)
            nc.vector.tensor_copy(chunk_base_i[:], small[0:1, P:P + CHUNKS]).then_inc(flag_ready, 1)
            nc.vector.tensor_copy(chunk_base[:], small[:, P:P + CHUNKS]).then_inc(flag_ready, 1)

            dve.wait_ge(bias_loaded, 64)
            nc.vector.tensor_scalar(eps1_col[:], eps_col[:], 1.0, None, ALU.add).then_inc(eps_ready, 1)
            for j, w_t in enumerate((w_edge_t, w1_t, w2_t)):
                dve.wait_ge(w_turned, 1)
                nc.vector.tensor_copy(w_t[0:F, :], ep[0][0:F, j * P:j * P + F]).then_inc(w_ready, 1)

            def add_half(t, s, h):
                pc, kc = shape_of(t)
                k0, k1 = h * HALF, min(kc, h * HALF + HALF)
                dve.wait_ge(projected, 2 * t + (h + 1))
                nc.vector.tensor_tensor(msg[s % 2][0:pc, k0:k1, :],
                                        ep[h][0:pc, 0:(k1 - k0) * F].rearrange("p (k f) -> p k f", f=F),
                                        x_src[s][0:pc, k0:k1, :], ALU.add).then_inc(added, 1)

            def take_dst(t, s, uses, base, to):
                pc, kc = shape_of(t)
                dve.wait_ge(dst_loaded[s], uses * 16)
                nc.vector.tensor_scalar(to[0:pc, 0:kc], dst_idx[s][0:pc, 0:kc], base[0:pc, :], None,
                                        ALU.subtract).then_inc(dst_taken, 1)

            def make_onehot(t):
                pc, kc = shape_of(t)
                nc.vector.tensor_tensor(onehot[0:pc, 0:kc, :],
                                        col_f[0:pc, :].unsqueeze(1).to_broadcast([pc, kc, W]),
                                        dst_rel[0:pc, 0:kc].unsqueeze(2).to_broadcast([pc, kc, W]),
                                        ALU.is_equal).then_inc(onehot_made, 1)

            def add_window(bank, node):
                nc.vector.tensor_tensor(sums_t[:, bass.ds(node, W)], sums_t[:, bass.ds(node, W)],
                                        win[bank][0:F, 0:W], ALU.add).then_inc(window_added, 1)

            def add_chunk(t, s, uses, windows):
                pc, kc = shape_of(t)
                dve.wait_ge(gathered[s], uses * (16 * K) - 16 * (K - kc))
                if not isinstance(t, int) or t >= 2:
                    dve.wait_ge(window_summed, t * windows - windows)
                add_half(t, s, 0)
                add_half(t, s, 1)

            def one_window(t, s, uses):
                loop = not isinstance(t, int)
                before = loop or t >= 1
                if before:
                    node = dve.value_load(chunk_base_i[0:1, bass.ds(t - 1, 1)], min_val=0, max_val=N - 1)
                    take_dst(t - 1, (s - 1) % SLOTS, uses if s else uses - 1,
                             chunk_base[:, bass.ds(t - 1, 1)], dst_rel)
                    if loop or t >= 2:
                        dve.wait_ge(window_summed, t - 1)
                    dve.wait_ge(dst_taken, t + 0)
                    make_onehot(t - 1)
                if loop or t < CHUNKS:
                    add_chunk(t, s, uses, 1)
                if before:
                    dve.wait_ge(window_summed, t + 0)
                    add_window((s - 1) % 2, node)

            def all_windows(t, s, uses):
                loop = not isinstance(t, int)
                before = loop or t >= 1
                if before:
                    take_dst(t - 1, (s - 1) % SLOTS, uses if s else uses - 1, window_base[:, 0:1], dst_f)
                if loop or t < CHUNKS:
                    add_chunk(t, s, uses, NB)
                if before:
                    with dve.Fori(0, NB) as w:
                        dve.wait_ge(dst_taken, t + 0)
                        n = (t - 1) * NB + w
                        pc, kc = shape_of(t - 1)
                        nc.vector.tensor_scalar(dst_rel[0:pc, 0:kc], dst_f[0:pc, 0:kc],
                                                window_base[0:pc, bass.ds(w, 1)], None,
                                                ALU.subtract).then_inc(rel_made, 1)
                        dve.wait_ge(rel_made, n + 1)
                        make_onehot(t - 1)
                        dve.wait_ge(window_summed, n + 1)
                        add_window(0, w * W)

            def chunks(step):
                for t in range(SLOTS):
                    step(t, t, 1)
                with dve.Fori(1, ROUNDS) as i:
                    for s in range(SLOTS):
                        step(i * SLOTS + s, s, i + 1)
                for t in range(ROUNDS * SLOTS, CHUNKS + 1):
                    step(t, t % SLOTS, t // SLOTS + 1)

            dve.wait_ge(sums_begun, GROUPS)
            dve.wait_ge(flag_ready, 3)
            spread = dve.value_load(spread_i[0:1, 0:1], min_val=0, max_val=2 * CHUNKS)
            with dve.If(spread == 0):
                chunks(one_window)
                dve.wait_ge(window_added, CHUNKS)
                dve.sem_inc(sums_done, 1)
            with dve.Else():
                chunks(all_windows)
                dve.wait_ge(window_added, CHUNKS * NB)
                dve.sem_inc(sums_done, 1)

            chain = 0
            for g in range(GROUPS + 1):
                if g < GROUPS:
                    n, pg, j = len(group_blocks[g]), group_rows[g], g % 2
                    dve.wait_ge(mlp_done, g + 1)
                    if g >= 2:
                        dve.wait_ge(y_ready, HALF * (g - 1))
                    nc.vector.tensor_tensor(res[j][0:pg, 0:n, :],
                                            ep[j][0:pg, 0:n * F].rearrange("p (k f) -> p k f", f=F),
                                            x_rows[0:pg, g * HALF:g * HALF + n, :], ALU.add).then_inc(res_ready, 1)
                    dve.wait_ge(res_ready, g + 1)
                    for b in range(n):
                        nc.vector.bn_stats(stats[0:pg, b, :], res[j][0:pg, b, :]).then_inc(norm_chain, 1)
                    chain += n
                    dve.wait_ge(norm_chain, chain)
                    for b in range(n):
                        nc.vector.bn_aggr(mean_var[j][0:pg, b, :], stats[0:pg, b, :]).then_inc(stats_ready, 1)
                if g >= 1:
                    n, pg, j = len(group_blocks[g - 1]), group_rows[g - 1], (g - 1) % 2
                    dve.wait_ge(std_ready, g)
                    nc.vector.reciprocal(rstd[j][0:pg, 0:n], std[j][0:pg, 0:n]).then_inc(norm_chain, 1)
                    chain += 1
                    dve.wait_ge(norm_chain, chain)
                    if g >= 3:
                        dve.wait_ge(stored[j], 16 * ((g - 1) // 2))
                    for b in range(n):
                        nc.vector.tensor_scalar(y[j][0:pg, b, :], res[j][0:pg, b, :], mean_var[j][0:pg, b, 0:1],
                                                rstd[j][0:pg, b:b + 1], ALU.subtract, ALU.mult).then_inc(y_ready, 1)

        @block.tensor
        def _(pe):
            pe.wait_ge(ident_made, 1)
            pe.wait_ge(weights_loaded, 48)
            for j in range(3):
                nc.tensor.transpose(ep[0][0:F, j * P:j * P + F], w_in[j][:], ident[0:F, 0:F]).then_inc(w_turned, 1)
            pe.wait_ge(consts, CONSTS)
            pe.wait_ge(flagged, 7)
            nc.tensor.matmul(small[0:1, 0:1], outside[:], ones[0:CHUNKS, :], start=True, stop=True)
            nc.tensor.matmul(small[:, P:P + CHUNKS], first_wide[:], ident[0:CHUNKS, 0:CHUNKS],
                             start=True, stop=True).then_inc(flag_summed, 1)
            pe.wait_ge(x_loaded, 32)
            for g, blocks in enumerate(group_blocks):
                if g >= 2:
                    pe.wait_ge(sums_begun, g - 1)
                for j, b in enumerate(blocks):
                    pb = block_nodes[b]
                    last = nc.tensor.transpose(tp[g % 2][0:F, j * P:j * P + pb], x_rows[0:pb, b, :],
                                               ident[0:pb, 0:pb])
                last.then_inc(x_turned, 1)
            pe.wait_ge(sums_begun, GROUPS)
            pe.wait_ge(w_ready, 3)
            pe.wait_ge(bias_loaded, 64)

            def messages(t, s, uses):
                pc, kc = shape_of(t)
                first = isinstance(t, int) and t == 0
                pe.wait_ge(attr_loaded[s], uses * 16)
                for h in range(2):
                    if not first:
                        pe.wait_ge(copied, 2 * t + (h - 1))
                    for k in range(h * HALF, min(kc, h * HALF + HALF)):
                        c = (k - h * HALF) * P
                        last = nc.tensor.transpose(tp[h][0:F, c:c + pc], attr[s][0:pc, k, :], ident[0:pc, 0:pc])
                    last.then_inc(turned, 1)
                for h in range(2):
                    pe.wait_ge(copied, 2 * t + (h + 1))
                    if not first:
                        pe.wait_ge(added, 2 * t + (h - 1))
                    for k in range(h * HALF, min(kc, h * HALF + HALF)):
                        j = k - h * HALF
                        last = nc.tensor.matmul(ep[h][0:pc, j * F:j * F + F], attr_t[h][:, j * P:j * P + pc],
                                                w_edge_t[:], start=True, stop=True)
                    last.then_inc(projected, 1)

            def sum_window(t, s, bank):
                pc, kc = shape_of(t)
                for k in range(kc):
                    last = nc.tensor.matmul(win[bank][0:F, 0:W], msg[s % 2][0:pc, k, :], onehot[0:pc, k, :],
                                            start=(k == 0), stop=(k == kc - 1))
                last.then_inc(window_summed, 1)

            def one_window(t, s, uses):
                loop = not isinstance(t, int)
                if loop or t < CHUNKS:
                    messages(t, s, uses)
                if loop or t >= 1:
                    pe.wait_ge(relued, 2 * t)
                    if loop or t >= 3:
                        pe.wait_ge(window_added, t - 2)
                    pe.wait_ge(onehot_made, t + 0)
                    sum_window(t - 1, (s - 1) % SLOTS, (s - 1) % 2)

            def all_windows(t, s, uses):
                loop = not isinstance(t, int)
                if loop or t < CHUNKS:
                    messages(t, s, uses)
                if loop or t >= 1:
                    with pe.Fori(0, NB) as w:
                        pe.wait_ge(relued, 2 * t)
                        pe.wait_ge(onehot_made, (t - 1) * NB + w + 1)
                        sum_window(t - 1, (s - 1) % SLOTS, 0)

            def chunks(step):
                for t in range(SLOTS):
                    step(t, t, 1)
                with pe.Fori(1, ROUNDS) as i:
                    for s in range(SLOTS):
                        step(i * SLOTS + s, s, i + 1)
                for t in range(ROUNDS * SLOTS, CHUNKS + 1):
                    step(t, t % SLOTS, t // SLOTS + 1)

            pe.wait_ge(flag_ready, 3)
            spread = pe.value_load(spread_i[0:1, 0:1], min_val=0, max_val=2 * CHUNKS)
            with pe.If(spread == 0):
                chunks(one_window)
            with pe.Else():
                chunks(all_windows)

            pe.wait_ge(sums_done, 1)
            for g in range(GROUPS + 1):
                if g < GROUPS:
                    if g >= 2:
                        pe.wait_ge(hid_ready, g - 1)
                    n = group_cols[g]
                    nc.tensor.matmul(tp[g % 2][0:F, 0:n], w1_t[:], sums_t[:, g * HALF * P:g * HALF * P + n],
                                     start=True, stop=True).then_inc(hid_done, 1)
                if g >= 1:
                    j = (g - 1) % 2
                    pe.wait_ge(hid_ready, g)
                    if g >= 3:
                        pe.wait_ge(res_ready, g - 2)
                    for b, blk in enumerate(group_blocks[g - 1]):
                        pb = block_nodes[blk]
                        last = nc.tensor.matmul(ep[j][0:pb, b * F:b * F + F], hid_t[j][:, b * P:b * P + pb],
                                                w2_t[:], start=True, stop=True)
                    last.then_inc(mlp_done, 1)


_INS = ["x", "src", "dst", "edge_attr_96", "L0_gnn_W_edge", "L0_gnn_b_edge", "L0_gnn_eps",
        "L0_gnn_W1", "L0_gnn_b1", "L0_gnn_W2", "L0_gnn_b2"]


def kernel(**inputs):
    import numpy as np
    import concourse.bacc as bacc
    from concourse import mybir as mb
    from concourse.bass_utils import run_bass_kernel_spmd

    nc = bacc.Bacc("TRN2", target_bir_lowering=False, num_devices=1)
    arrays, args = {}, []
    for name in _INS:
        a = np.ascontiguousarray(inputs[name])
        arrays["in_" + name] = a
        args.append(nc.dram_tensor("in_" + name, a.shape, mb.dt.from_np(a.dtype), kind="ExternalInput").ap())
    out = nc.dram_tensor("out", arrays["in_x"].shape, F32, kind="ExternalOutput").ap()
    build_gnn(nc, *args, out)
    r = run_bass_kernel_spmd(nc, [arrays], core_ids=[0])
    return r.results[0]["out"]
```

```python
from contextlib import ExitStack

import concourse.bass as bass
from concourse import mybir

F32 = mybir.dt.float32
I32 = mybir.dt.int32
ALU = mybir.AluOpType
ACT = mybir.ActivationFunctionType
AX_X = mybir.AxisListType.X

P = 128
K = 8
HALF = 4
W = 96
SLOTS = 6
LN_EPS = 1e-5


def build_gnn(nc, x, src, dst, edge_attr, w_edge, b_edge, eps, w1, b1, w2, b2, out):
    N, F = x.shape
    E = src.shape[0]
    CHUNK = P * K
    FULL = E // CHUNK
    REST = E - FULL * CHUNK
    KL = 6
    PL = REST // KL
    CHUNKS = FULL + 1
    ROUNDS = FULL // SLOTS
    assert PL * KL == REST and PL <= P and PL % 16 == 0 and CHUNKS <= P
    NB = -(-N // W)
    XT = N // P
    XREST = N - P * XT
    XGROUPS = XT // HALF
    PAIRS = (NB - 1) // 2
    assert CHUNKS % 2 == 0
    assert XGROUPS * HALF == XT and SLOTS % 2 == 0 and 3 <= SLOTS and ROUNDS * SLOTS <= FULL
    TAIL = N - W

    def shape_of(t):
        return (PL, KL) if isinstance(t, int) and t == CHUNKS - 1 else (P, K)

    def within(t, low, high):
        return not isinstance(t, int) or low <= t < high

    def since(v, low):
        return not isinstance(v, int) or v >= low

    def steps(eng, step, last):
        for t in range(SLOTS):
            step(t, t, 1)
        with eng.Fori(1, ROUNDS) as i:
            for s in range(SLOTS):
                step(i * SLOTS + s, s, i + 1)
        for t in range(ROUNDS * SLOTS, last):
            step(t, t % SLOTS, t // SLOTS + 1)

    def all_nodes(eng, node_pass, v0):
        node_pass(v0, 0, 0)
        node_pass(v0 + 1, 1, W)
        with eng.Fori(1, PAIRS) as q:
            for j in range(2):
                node_pass(q * 2 + (v0 + j), j, q * (2 * W) + j * W)
        for w in range(2 * PAIRS, NB):
            node_pass(v0 + w, w % 2, min(w * W, TAIL))

    with ExitStack() as ctx:
        def sb(name, shape, dt=F32):
            return ctx.enter_context(nc.sbuf_tensor(name, shape, dt))

        def ps(name, shape=(P, 512)):
            return ctx.enter_context(nc.psum_tensor(name, list(shape), F32))

        def sem(name):
            return ctx.enter_context(nc.semaphore(name))

        src_idx = [sb(f"src_idx{s}", [P, K], I32) for s in range(SLOTS)]
        dst_idx = [sb(f"dst_idx{s}", [P, K], I32) for s in range(SLOTS)]
        attr = [sb(f"attr{s}", [P, K, F]) for s in range(SLOTS)]
        x_src = [sb(f"x_src{s}", [P, K, F]) for s in range(SLOTS)]
        attr_t = [sb(f"attr_t{h}", [F + 1, HALF * P]) for h in range(2)]
        msg = [sb(f"msg{m}", [P, K, F]) for m in range(2)]
        dst_f = sb("dst_f", [P, K])
        dst_rel = sb("dst_rel", [P, K])
        onehot = sb("onehot", [P, K, W])
        sums_t = sb("sums_t", [F, NB * W])
        x_rows = sb("x_rows", [P, XT, F])
        x_rest = sb("x_rest", [P, F])
        dst_rows = sb("dst_rows", [CHUNKS, CHUNK], I32)
        lowest = sb("lowest", [CHUNKS, 1])
        highest = sb("highest", [CHUNKS, 1])
        base_wide = sb("base_wide", [CHUNKS, P])
        span = sb("span", [CHUNKS, 1])
        outside = sb("outside", [CHUNKS, 1])
        chunk_base = sb("chunk_base", [P, CHUNKS])
        chunk_base_i = sb("chunk_base_i", [1, CHUNKS], I32)
        base_steps = sb("base_steps", [1, CHUNKS + 1])
        widest = sb("widest", [1, 1])
        uncovered = sb("uncovered", [1, 1])
        spread_i = sb("spread_i", [1, 1], I32)
        uncovered_i = sb("uncovered_i", [1, 1], I32)
        window_base_i = sb("window_base_i", [P, NB], I32)
        window_base = sb("window_base", [P, NB])
        col_i = sb("col_i", [P, P], I32)
        row_i = sb("row_i", [P, 1], I32)
        ident = sb("ident", [P, P])
        ones = sb("ones", [P, 1])
        w_in = [sb(f"w_in{j}", [F, F]) for j in range(3)]
        w_edge_t = sb("w_edge_t", [F + 1, F])
        w1_t = sb("w1_t", [F, F])
        w2_t = sb("w2_t", [F + 1, F])
        b1_col = sb("b1_col", [F, 1])
        eps_col = sb("eps_col", [F, 1])
        eps1_col = sb("eps1_col", [F, 1])
        x_win = [sb(f"x_win{j}", [W, F]) for j in range(2)]
        hid_t = sb("hid_t", [F + 1, W])
        res = [sb(f"res{j}", [W, F]) for j in range(2)]
        stats = sb("stats", [W, 6])
        mean_var = [sb(f"mean_var{j}", [W, 2]) for j in range(2)]
        ln_eps = sb("ln_eps", [W, 1])
        std = [sb(f"std{j}", [W, 1]) for j in range(2)]
        rstd = [sb(f"rstd{j}", [W, 1]) for j in range(2)]
        y = [sb(f"y{j}", [W, F]) for j in range(2)]

        tp = [ps(f"tp{h}") for h in range(2)]
        ep = [ps(f"ep{h}") for h in range(2)]
        win = ps("win")
        hid = ps("hid")
        mlp = ps("mlp")
        col_f = ps("col_f", (P, P))

        src_loaded = [sem(f"src_loaded{s}") for s in range(SLOTS)]
        dst_loaded = [sem(f"dst_loaded{s}") for s in range(SLOTS)]
        attr_loaded = [sem(f"attr_loaded{s}") for s in range(SLOTS)]
        gathered = [sem(f"gathered{s}") for s in range(SLOTS)]
        sp_steps = sem("sp_steps")
        pool_steps = sem("pool_steps")
        act_steps = sem("act_steps")
        dve_steps = sem("dve_steps")
        pe_steps = sem("pe_steps")
        rows_loaded = sem("rows_loaded")
        weights_loaded = sem("weights_loaded")
        bias_loaded = sem("bias_loaded")
        x_loaded = sem("x_loaded")
        iotas_made = sem("iotas_made")
        consts = sem("consts")
        ident_made = sem("ident_made")
        checked = sem("checked")
        check_summed = sem("check_summed")
        check_ready = sem("check_ready")
        w_turned = sem("w_turned")
        w_ready = sem("w_ready")
        eps_ready = sem("eps_ready")
        x_turned = sem("x_turned")
        sums_begun = sem("sums_begun")
        turned = sem("turned")
        copied = sem("copied")
        projected = sem("projected")
        added = sem("added")
        relued = sem("relued")
        dst_taken = sem("dst_taken")
        rel_made = sem("rel_made")
        onehot_made = sem("onehot_made")
        window_summed = sem("window_summed")
        window_added = sem("window_added")
        x_win_loaded = [sem(f"x_win_loaded{j}") for j in range(2)]
        hid_done = sem("hid_done")
        hid_ready = sem("hid_ready")
        mlp_done = sem("mlp_done")
        res_ready = sem("res_ready")
        stats_made = sem("stats_made")
        mean_ready = sem("mean_ready")
        std_ready = sem("std_ready")
        rstd_ready = sem("rstd_ready")
        y_ready = sem("y_ready")
        stored = sem("stored")

        CHECKS = 4
        CONSTS = 8
        LAST_START = E - CHUNK
        BASES = slice(P, P + CHUNKS)

        block = ctx.enter_context(nc.Block())

        @block.sync
        def _(sp):
            def load(start, s, pc, kc):
                n = pc * kc
                sp.dma_start(src_idx[s][0:pc, 0:kc],
                             src[bass.ds(start, n)].rearrange("(p k) -> p k", k=kc)).then_inc(src_loaded[s], 16)
                sp.dma_start(dst_idx[s][0:pc, 0:kc],
                             dst[bass.ds(start, n)].rearrange("(p k) -> p k", k=kc)).then_inc(dst_loaded[s], 16)
                sp.dma_start(attr[s][0:pc, 0:kc, :],
                             edge_attr[bass.ds(start, n), :].rearrange("(p k) f -> p k f", k=kc)
                             ).then_inc(attr_loaded[s], 16)

            for s in range(SLOTS):
                load(s * CHUNK, s, P, K)
            with sp.Fori(1, ROUNDS) as i:
                for s in range(SLOTS):
                    start = sp.snap(i * (SLOTS * CHUNK) + s * CHUNK)
                    sp.wait_ge(gathered[s], i * (16 * K))
                    sp.sem_inc(sp_steps, 1)
                    sp.wait_ge(turned, i * (2 * SLOTS) + (2 * (s - SLOTS) + 2))
                    sp.sem_inc(sp_steps, 1)
                    sp.wait_ge(dst_taken, i * SLOTS + (s - SLOTS + 1))
                    sp.sem_inc(sp_steps, 1)
                    load(start, s, P, K)
            for t in range(ROUNDS * SLOTS, CHUNKS):
                s, u = t % SLOTS, t - SLOTS
                sp.wait_ge(gathered[s], 16 * K * (t // SLOTS))
                sp.wait_ge(turned, 2 * u + 2)
                sp.wait_ge(dst_taken, u + 1)
                load(t * CHUNK, s, *shape_of(t))

        @block.gpsimd
        def _(pool):
            nc.gpsimd.iota(col_i[:], pattern=[[1, P]], base=0, channel_multiplier=0).then_inc(iotas_made, 1)
            nc.gpsimd.iota(row_i[:], pattern=[[0, 1]], base=0, channel_multiplier=1).then_inc(iotas_made, 1)
            nc.gpsimd.iota(window_base_i[:], pattern=[[W, NB]], base=0, channel_multiplier=0).then_inc(iotas_made, 1)

            def gather(s, pc, kc):
                for k in range(kc):
                    nc.gpsimd.indirect_dma_start(
                        out=x_src[s][0:pc, k, :], out_offset=None, in_=x,
                        in_offset=bass.IndirectOffsetOnAxis(ap=src_idx[s][0:pc, k:k + 1], axis=0),
                    ).then_inc(gathered[s], 16)

            for s in range(SLOTS):
                pool.wait_ge(src_loaded[s], 16)
                gather(s, P, K)
            with pool.Fori(1, ROUNDS) as i:
                for s in range(SLOTS):
                    pool.wait_ge(added, i * (2 * SLOTS) + (2 * (s - SLOTS) + 2))
                    pool.wait_ge(src_loaded[s], i * 16 + 16)
                    pool.sem_inc(pool_steps, 1)
                    gather(s, P, K)
            for t in range(ROUNDS * SLOTS, CHUNKS):
                s = t % SLOTS
                pool.wait_ge(added, 2 * (t - SLOTS) + 2)
                pool.wait_ge(src_loaded[s], 16 * (t // SLOTS + 1))
                gather(s, *shape_of(t))

        @block.scalar
        def _(act):
            act.dma_start(dst_rows[0:FULL, :], dst[0:FULL * CHUNK].rearrange("(t e) -> t e", e=CHUNK)
                          ).then_inc(rows_loaded, 16)
            act.dma_start(dst_rows[FULL:CHUNKS, :], dst[LAST_START:E].rearrange("(t e) -> t e", e=CHUNK)
                          ).then_inc(rows_loaded, 16)
            for j, w in enumerate((w_edge, w1, w2)):
                act.dma_start(w_in[j][:], w).then_inc(weights_loaded, 16)
            act.dma_start(w_edge_t[F:F + 1, :], b_edge.rearrange("(a f) -> a f", a=1)).then_inc(bias_loaded, 16)
            act.dma_start(w2_t[F:F + 1, :], b2.rearrange("(a f) -> a f", a=1)).then_inc(bias_loaded, 16)
            act.dma_start(b1_col[:], b1.rearrange("(f a) -> f a", a=1)).then_inc(bias_loaded, 16)
            act.dma_start(eps_col[:], eps.rearrange("(a b) -> a b", a=1).to_broadcast([F, 1])
                          ).then_inc(bias_loaded, 16)
            act.dma_start(x_rows[:], x[0:P * XT, :].rearrange("(p j) f -> p j f", j=XT)).then_inc(x_loaded, 16)
            act.dma_start(x_rest[0:XREST, :], x[P * XT:N, :]).then_inc(x_loaded, 16)

            act.wait_ge(eps_ready, 1)
            by_tile = sums_t[:, 0:P * XT].rearrange("f (p j) -> f j p", j=XT)
            for g in range(XGROUPS + 1):
                act.wait_ge(x_turned, g + 1)
                if g < XGROUPS:
                    to = by_tile[:, g * HALF:g * HALF + HALF, :]
                    of = tp[g % 2][0:F, :].rearrange("f (j p) -> f j p", p=P)
                else:
                    to, of = sums_t[:, P * XT:N], tp[g % 2][0:F, 0:XREST]
                nc.scalar.activation(to, of, ACT.Copy, scale=eps1_col[:, 0:1]).then_inc(sums_begun, 1)

            def copy_half(t, h):
                pc, kc = shape_of(t)
                n = min(kc - h * HALF, HALF)
                act.wait_ge(turned, 2 * t + (h + 1))
                if within(t, 1, CHUNKS):
                    act.wait_ge(projected, 2 * t + (h - 1))
                nc.scalar.activation(
                    attr_t[h][0:F, :].rearrange("f (k p) -> f k p", p=P)[:, 0:n, 0:pc],
                    tp[h][0:F, :].rearrange("f (k p) -> f k p", p=P)[:, 0:n, 0:pc],
                    ACT.Copy).then_inc(copied, 1)

            def relu_half(t, s, h):
                pc, kc = shape_of(t)
                half = msg[s % 2][0:pc, h * HALF:min(kc, h * HALF + HALF), :]
                act.wait_ge(added, 2 * t + (h + 1))
                nc.scalar.activation(half, half, ACT.Relu).then_inc(relued, 1)

            def hidden(v):
                act.wait_ge(hid_done, v + 1)
                if since(v, 1):
                    act.wait_ge(mlp_done, v + 0)
                nc.scalar.activation(hid_t[0:F, :], hid[0:F, 0:W], ACT.Relu, bias=b1_col[:, 0:1]
                                     ).then_inc(hid_ready, 1)

            def root(v, j):
                act.wait_ge(mean_ready, v + 1)
                nc.scalar.activation(std[j][:], mean_var[j][:, 1:2], ACT.Sqrt, bias=ln_eps[:, 0:1]
                                     ).then_inc(std_ready, 1)

            def load_x(v, j, node):
                if since(v, 2):
                    act.wait_ge(res_ready, v - 1)
                    act.sem_inc(act_steps, 1)
                act.dma_start(x_win[j][:], x[bass.ds(node, W), :]).then_inc(x_win_loaded[j], 16)

            def store(v, j, node):
                act.wait_ge(y_ready, v + 1)
                act.sem_inc(act_steps, 1)
                if since(v, 1):
                    act.wait_ge(stored, v * 16)
                    act.sem_inc(act_steps, 1)
                act.dma_start(out[bass.ds(node, W), :], y[j][:]).then_inc(stored, 16)

            def base(v):
                return act.value_load(chunk_base_i[0:1, bass.ds(v, 1)], min_val=0, max_val=TAIL)

            def one_window(t, s, uses):
                if within(t, 3, CHUNKS + 3):
                    root(t - 3, (s - 3) % 2)
                if within(t, 2, CHUNKS + 2):
                    hidden(t - 2)
                if within(t, 0, CHUNKS):
                    copy_half(t, 0)
                    copy_half(t, 1)
                if within(t, 1, CHUNKS + 1):
                    relu_half(t - 1, (s - 1) % SLOTS, 0)
                    relu_half(t - 1, (s - 1) % SLOTS, 1)
                    load_x(t - 1, (s - 1) % 2, base(t - 1))
                if within(t, 3, CHUNKS + 3):
                    store(t - 3, (s - 3) % 2, base(t - 3))

            def all_windows(t, s, uses):
                if within(t, 0, CHUNKS):
                    copy_half(t, 0)
                    copy_half(t, 1)
                if within(t, 1, CHUNKS + 1):
                    relu_half(t - 1, (s - 1) % SLOTS, 0)
                    relu_half(t - 1, (s - 1) % SLOTS, 1)

            def node_pass(v, j, node):
                load_x(v, j, node)
                hidden(v)
                root(v, j)
                store(v, j, node)

            act.wait_ge(check_ready, CHECKS)
            spread = act.value_load(spread_i[0:1, 0:1], min_val=0, max_val=CHUNKS)
            missing = act.value_load(uncovered_i[0:1, 0:1], min_val=0, max_val=3)
            with act.If(spread == 0):
                steps(act, one_window, CHUNKS + 3)
                with act.If(missing != 0):
                    all_nodes(act, node_pass, CHUNKS)
                    act.wait_ge(stored, 16 * (CHUNKS + NB))
                    act.sem_inc(act_steps, 1)
                act.wait_ge(stored, 16 * CHUNKS)
                act.sem_inc(act_steps, 1)
            with act.Else():
                steps(act, all_windows, CHUNKS + 1)
                all_nodes(act, node_pass, 0)
                act.wait_ge(stored, 16 * NB)
                act.sem_inc(act_steps, 1)

        @block.vector
        def _(dve):
            nc.vector.memset(ones[:], 1.0).then_inc(consts, 1)
            nc.vector.memset(ln_eps[:], LN_EPS).then_inc(consts, 1)
            for a in (attr_t[0], attr_t[1], hid_t):
                nc.vector.memset(a[F:F + 1, :], 1.0).then_inc(consts, 1)
            if NB * W > N:
                nc.vector.memset(sums_t[:, N:NB * W], 0.0).then_inc(consts, 1)
            dve.wait_ge(iotas_made, 3)
            nc.vector.tensor_tensor(ident[:], col_i[:], row_i[:].to_broadcast([P, P]),
                                    ALU.is_equal).then_inc(ident_made, 1)
            nc.vector.tensor_copy(col_f[:], col_i[:]).then_inc(consts, 1)
            nc.vector.tensor_copy(window_base[:], window_base_i[:]).then_inc(consts, 1)

            dve.wait_ge(rows_loaded, 32)
            nc.vector.tensor_reduce(lowest[:], dst_rows[:], AX_X, ALU.min).then_inc(checked, 1)
            nc.vector.tensor_reduce(highest[:], dst_rows[:], AX_X, ALU.max).then_inc(checked, 1)
            dve.wait_ge(checked, 2)
            nc.vector.tensor_scalar(base_wide[:], lowest[:].to_broadcast([CHUNKS, P]), float(TAIL), None,
                                    ALU.min).then_inc(checked, 1)
            dve.wait_ge(checked, 3)
            nc.vector.tensor_tensor(span[:], highest[:], base_wide[:, 0:1], ALU.subtract).then_inc(checked, 1)
            dve.wait_ge(checked, 4)
            nc.vector.tensor_scalar(outside[:], span[:], float(W - 1), None, ALU.is_gt).then_inc(checked, 1)
            dve.wait_ge(check_summed, 1)
            nc.vector.tensor_copy(spread_i[:], win[0:1, 0:1]).then_inc(check_ready, 1)
            nc.vector.tensor_copy(chunk_base_i[:], win[0:1, BASES]).then_inc(check_ready, 1)
            nc.vector.tensor_copy(chunk_base[:], win[:, BASES]).then_inc(check_ready, 1)
            dve.wait_ge(check_ready, 3)
            nc.vector.tensor_tensor(base_steps[:, 1:CHUNKS], chunk_base[0:1, 1:CHUNKS],
                                    chunk_base[0:1, 0:CHUNKS - 1], ALU.subtract).then_inc(checked, 1)
            nc.vector.tensor_scalar(base_steps[:, 0:1], chunk_base[0:1, 0:1], float(W), None,
                                    ALU.add).then_inc(checked, 1)
            nc.vector.tensor_scalar(base_steps[:, CHUNKS:CHUNKS + 1], chunk_base[0:1, CHUNKS - 1:CHUNKS],
                                    -1.0, float(TAIL + W), ALU.mult, ALU.add).then_inc(checked, 1)
            dve.wait_ge(checked, 8)
            nc.vector.tensor_reduce(widest[:], base_steps[:], AX_X, ALU.max).then_inc(checked, 1)
            dve.wait_ge(checked, 9)
            nc.vector.tensor_scalar(uncovered_i[:], widest[:], float(W), None, ALU.is_gt).then_inc(check_ready, 1)

            dve.wait_ge(bias_loaded, 64)
            nc.vector.tensor_scalar(eps1_col[:], eps_col[:], 1.0, None, ALU.add).then_inc(eps_ready, 1)
            dve.wait_ge(w_turned, 3)
            for j, w_t in enumerate((w_edge_t, w1_t, w2_t)):
                nc.vector.tensor_copy(w_t[0:F, :], ep[0][0:F, j * P:j * P + F]).then_inc(w_ready, 1)

            def add_half(t, s, h):
                pc, kc = shape_of(t)
                k0, k1 = h * HALF, min(kc, h * HALF + HALF)
                dve.wait_ge(projected, 2 * t + (h + 1))
                nc.vector.tensor_tensor(msg[s % 2][0:pc, k0:k1, :],
                                        ep[h][0:pc, 0:(k1 - k0) * F].rearrange("p (k f) -> p k f", f=F),
                                        x_src[s][0:pc, k0:k1, :], ALU.add).then_inc(added, 1)

            def take_dst(t, s, uses, base, to):
                pc, kc = shape_of(t)
                dve.wait_ge(dst_loaded[s], uses * 16)
                nc.vector.tensor_scalar(to[0:pc, 0:kc], dst_idx[s][0:pc, 0:kc], base[0:pc, :], None,
                                        ALU.subtract).then_inc(dst_taken, 1)

            def make_onehot(t):
                pc, kc = shape_of(t)
                nc.vector.tensor_tensor(onehot[0:pc, 0:kc, :],
                                        col_f[0:pc, 0:W].unsqueeze(1).to_broadcast([pc, kc, W]),
                                        dst_rel[0:pc, 0:kc].unsqueeze(2).to_broadcast([pc, kc, W]),
                                        ALU.is_equal).then_inc(onehot_made, 1)

            def add_window(node):
                nc.vector.tensor_tensor(sums_t[:, bass.ds(node, W)], sums_t[:, bass.ds(node, W)],
                                        win[0:F, 0:W], ALU.add).then_inc(window_added, 1)

            def add_chunk(t, s, uses, windows):
                pc, kc = shape_of(t)
                dve.wait_ge(gathered[s], uses * (16 * K) - 16 * (K - kc))
                if within(t, 2, CHUNKS):
                    dve.wait_ge(window_summed, t * windows - windows)
                add_half(t, s, 0)
                add_half(t, s, 1)

            def residual(v, j):
                dve.wait_ge(mlp_done, v + 1)
                dve.wait_ge(x_win_loaded[j], v * 8 + (16 - 8 * j))
                if since(v, 2):
                    dve.wait_ge(y_ready, v - 1)
                nc.vector.tensor_tensor(res[j][:], mlp[0:W, 0:F], x_win[j][:], ALU.add).then_inc(res_ready, 1)
                dve.wait_ge(res_ready, v + 1)
                if since(v, 1):
                    dve.wait_ge(mean_ready, v + 0)
                nc.vector.bn_stats(stats[:], res[j][:]).then_inc(stats_made, 1)
                dve.wait_ge(stats_made, v + 1)
                dve.sem_inc(dve_steps, 1)
                nc.vector.bn_aggr(mean_var[j][:], stats[:]).then_inc(mean_ready, 1)

            def norm(v, j):
                dve.wait_ge(std_ready, v + 1)
                nc.vector.reciprocal(rstd[j][:], std[j][:]).then_inc(rstd_ready, 1)
                dve.wait_ge(rstd_ready, v + 1)
                if since(v, 2):
                    dve.wait_ge(stored, v * 16 - 16)
                nc.vector.tensor_scalar(y[j][:], res[j][:], mean_var[j][:, 0:1], rstd[j][:, 0:1],
                                        ALU.subtract, ALU.mult).then_inc(y_ready, 1)

            def one_window(t, s, uses):
                before = within(t, 1, CHUNKS + 1)
                if before:
                    node = dve.value_load(chunk_base_i[0:1, bass.ds(t - 1, 1)], min_val=0, max_val=TAIL)
                if within(t, 3, CHUNKS + 3):
                    norm(t - 3, (s - 3) % 2)
                if before:
                    take_dst(t - 1, (s - 1) % SLOTS, uses if s else uses - 1,
                             chunk_base[:, bass.ds(t - 1, 1)], dst_rel)
                    if within(t, 2, CHUNKS + 1):
                        dve.wait_ge(window_summed, t - 1)
                    dve.wait_ge(dst_taken, t + 0)
                    make_onehot(t - 1)
                if within(t, 0, CHUNKS):
                    add_chunk(t, s, uses, 1)
                if before:
                    dve.wait_ge(window_summed, t + 0)
                    if within(t, 2, CHUNKS + 1):
                        dve.wait_ge(window_added, t - 1)
                    add_window(node)
                if within(t, 2, CHUNKS + 2):
                    residual(t - 2, (s - 2) % 2)

            def all_windows(t, s, uses):
                before = within(t, 1, CHUNKS + 1)
                if before:
                    take_dst(t - 1, (s - 1) % SLOTS, uses if s else uses - 1, window_base[:, 0:1], dst_f)
                if within(t, 0, CHUNKS):
                    add_chunk(t, s, uses, NB)
                if before:
                    with dve.Fori(0, NB) as w:
                        dve.wait_ge(dst_taken, t + 0)
                        n = (t - 1) * NB + w
                        pc, kc = shape_of(t - 1)
                        nc.vector.tensor_scalar(dst_rel[0:pc, 0:kc], dst_f[0:pc, 0:kc],
                                                window_base[0:pc, bass.ds(w, 1)], None,
                                                ALU.subtract).then_inc(rel_made, 1)
                        dve.wait_ge(rel_made, n + 1)
                        make_onehot(t - 1)
                        dve.wait_ge(window_summed, n + 1)
                        add_window(w * W)

            def node_pass(v, j, node):
                residual(v, j)
                norm(v, j)

            dve.wait_ge(sums_begun, XGROUPS + 1)
            dve.wait_ge(check_ready, CHECKS)
            spread = dve.value_load(spread_i[0:1, 0:1], min_val=0, max_val=CHUNKS)
            missing = dve.value_load(uncovered_i[0:1, 0:1], min_val=0, max_val=3)
            with dve.If(spread == 0):
                steps(dve, one_window, CHUNKS + 3)
                with dve.If(missing != 0):
                    all_nodes(dve, node_pass, CHUNKS)
                dve.wait_ge(y_ready, CHUNKS)
                dve.sem_inc(dve_steps, 1)
            with dve.Else():
                steps(dve, all_windows, CHUNKS + 1)
                all_nodes(dve, node_pass, 0)

        @block.tensor
        def _(pe):
            pe.wait_ge(ident_made, 1)
            pe.wait_ge(weights_loaded, 48)
            for j in range(3):
                nc.tensor.transpose(ep[0][0:F, j * P:j * P + F], w_in[j][:], ident[0:F, 0:F]).then_inc(w_turned, 1)
            pe.wait_ge(consts, CONSTS)
            pe.wait_ge(checked, 5)
            nc.tensor.matmul(win[0:1, 0:1], outside[:], ones[0:CHUNKS, :], start=True, stop=True)
            nc.tensor.matmul(win[:, BASES], base_wide[:], ident[0:CHUNKS, 0:CHUNKS],
                             start=True, stop=True).then_inc(check_summed, 1)
            pe.wait_ge(x_loaded, 32)
            for g in range(XGROUPS + 1):
                if g >= 2:
                    pe.wait_ge(sums_begun, g - 1)
                if g < XGROUPS:
                    for j in range(HALF):
                        last = nc.tensor.transpose(tp[g % 2][0:F, j * P:j * P + P], x_rows[:, g * HALF + j, :],
                                                   ident[:])
                else:
                    last = nc.tensor.transpose(tp[g % 2][0:F, 0:XREST], x_rest[0:XREST, :],
                                               ident[0:XREST, 0:XREST])
                last.then_inc(x_turned, 1)
            pe.wait_ge(sums_begun, XGROUPS + 1)
            pe.wait_ge(w_ready, 3)
            pe.wait_ge(bias_loaded, 64)

            def messages(t, s, uses):
                pc, kc = shape_of(t)
                pe.wait_ge(attr_loaded[s], uses * 16)
                for h in range(2):
                    if within(t, 1, CHUNKS):
                        pe.wait_ge(copied, 2 * t + (h - 1))
                    for k in range(h * HALF, min(kc, h * HALF + HALF)):
                        c = (k - h * HALF) * P
                        last = nc.tensor.transpose(tp[h][0:F, c:c + pc], attr[s][0:pc, k, :], ident[0:pc, 0:pc])
                    last.then_inc(turned, 1)
                for h in range(2):
                    pe.wait_ge(copied, 2 * t + (h + 1))
                    if within(t, 1, CHUNKS):
                        pe.wait_ge(added, 2 * t + (h - 1))
                    for k in range(h * HALF, min(kc, h * HALF + HALF)):
                        j = k - h * HALF
                        last = nc.tensor.matmul(ep[h][0:pc, j * F:j * F + F], attr_t[h][:, j * P:j * P + pc],
                                                w_edge_t[:], start=True, stop=True)
                    last.then_inc(projected, 1)

            def sum_window(t, s):
                pc, kc = shape_of(t)
                for k in range(kc):
                    last = nc.tensor.matmul(win[0:F, 0:W], msg[s % 2][0:pc, k, :], onehot[0:pc, k, :],
                                            start=(k == 0), stop=(k == kc - 1))
                last.then_inc(window_summed, 1)

            def hidden(v, node):
                if since(v, 1):
                    pe.wait_ge(hid_ready, v + 0)
                nc.tensor.matmul(hid[0:F, 0:W], w1_t[:], sums_t[:, bass.ds(node, W)],
                                 start=True, stop=True).then_inc(hid_done, 1)

            def output(v):
                pe.wait_ge(hid_ready, v + 1)
                if since(v, 1):
                    pe.wait_ge(res_ready, v + 0)
                nc.tensor.matmul(mlp[0:W, 0:F], hid_t[:], w2_t[:], start=True, stop=True).then_inc(mlp_done, 1)

            def one_window(t, s, uses):
                if within(t, 2, CHUNKS + 2):
                    node = pe.value_load(chunk_base_i[0:1, bass.ds(t - 2, 1)], min_val=0, max_val=TAIL)
                    pe.wait_ge(window_added, t - 1)
                    hidden(t - 2, node)
                if within(t, 0, CHUNKS):
                    messages(t, s, uses)
                if within(t, 1, CHUNKS + 1):
                    pe.wait_ge(relued, 2 * t)
                    if within(t, 2, CHUNKS + 1):
                        pe.wait_ge(window_added, t - 1)
                    pe.wait_ge(onehot_made, t + 0)
                    sum_window(t - 1, (s - 1) % SLOTS)
                if within(t, 2, CHUNKS + 2):
                    output(t - 2)

            def all_windows(t, s, uses):
                if within(t, 0, CHUNKS):
                    messages(t, s, uses)
                if within(t, 1, CHUNKS + 1):
                    with pe.Fori(0, NB) as w:
                        pe.wait_ge(relued, 2 * t)
                        pe.wait_ge(onehot_made, (t - 1) * NB + w + 1)
                        sum_window(t - 1, (s - 1) % SLOTS)

            def node_pass(v, j, node):
                hidden(v, node)
                output(v)

            pe.wait_ge(check_ready, CHECKS)
            spread = pe.value_load(spread_i[0:1, 0:1], min_val=0, max_val=CHUNKS)
            missing = pe.value_load(uncovered_i[0:1, 0:1], min_val=0, max_val=3)
            with pe.If(spread == 0):
                steps(pe, one_window, CHUNKS + 3)
                with pe.If(missing != 0):
                    all_nodes(pe, node_pass, CHUNKS)
                pe.wait_ge(mlp_done, CHUNKS)
                pe.sem_inc(pe_steps, 1)
            with pe.Else():
                steps(pe, all_windows, CHUNKS + 1)
                pe.wait_ge(window_added, CHUNKS * NB)
                all_nodes(pe, node_pass, 0)


_INS = ["x", "src", "dst", "edge_attr_96", "L0_gnn_W_edge", "L0_gnn_b_edge", "L0_gnn_eps",
        "L0_gnn_W1", "L0_gnn_b1", "L0_gnn_W2", "L0_gnn_b2"]


def kernel(**inputs):
    import numpy as np
    import concourse.bacc as bacc
    from concourse import mybir as mb
    from concourse.bass_utils import run_bass_kernel_spmd

    nc = bacc.Bacc("TRN2", target_bir_lowering=False, num_devices=1)
    arrays, args = {}, []
    for name in _INS:
        a = np.ascontiguousarray(inputs[name])
        arrays["in_" + name] = a
        args.append(nc.dram_tensor("in_" + name, a.shape, mb.dt.from_np(a.dtype), kind="ExternalInput").ap())
    out = nc.dram_tensor("out", arrays["in_x"].shape, F32, kind="ExternalOutput").ap()
    build_gnn(nc, *args, out)
    r = run_bass_kernel_spmd(nc, [arrays], core_ids=[0])
    return r.results[0]["out"]
```
